# Optimizing a Trainium2 kernel written in Bass

```python
import numpy as np
import jax
import jax.numpy as jnp

def _softmax(x, axis=-1):
    return jax.nn.softmax(x, axis=axis)

def _gelu(x):
    return jax.nn.gelu(x, approximate=True)

def _silu(x):
    return jax.nn.silu(x)

def _sigmoid(x):
    return jax.nn.sigmoid(x)

def _layernorm(x, axis=-1, eps=1e-05):
    m = jnp.mean(x, axis=axis, keepdims=True)
    v = jnp.var(x, axis=axis, keepdims=True)
    return (x - m) / jnp.sqrt(v + eps)

def _scatter_add(tgt, idx, src, axis=0):
    return tgt.at[idx].add(src)

def _segment_sum(src, seg, n):
    return jax.ops.segment_sum(src, seg, n)
kernel_name = 'mk_adj_seq_d4_adj_r2_502f45'

def setup_inputs(seed: int=0):
    np.random.seed(seed)
    _w = jnp.asarray

    def _rec_inputs():
        import jax
        import jax.numpy as jnp
        _gk = jax.random.key(seed)
        x = -0.0002928 + 1 * jax.random.normal(jax.random.fold_in(_gk, 1), (32, 256, 256), jnp.float32)
        _a = jax.random.bernoulli(jax.random.fold_in(_gk, 2), 0.015625, (32, 256, 256))
        _a = jnp.logical_or(_a, jnp.swapaxes(_a, -1, -2))
        _a = jnp.logical_or(_a, jnp.eye(256, dtype=bool))
        _af = _a.astype(jnp.float32)
        adj = _af
        return (x, adj)
    x, adj = _rec_inputs()

    def _L0_gnn_setup():
        import jax, jax.numpy as jnp
        import numpy as np
        D_MODEL = 256
        N_HEADS = 8
        D_HEAD = D_MODEL // N_HEADS
        B = 8
        N = 512
        EPS = 1e-05
        key = jax.random.key(seed)
        ks = jax.random.split(key, 12)
        x = jax.random.normal(ks[0], (B, N, D_MODEL), dtype=jnp.float32)
        adj = (jax.random.uniform(ks[1], (B, N, N)) < 0.05).astype(jnp.float32)
        s = 1.0 / np.sqrt(D_MODEL)

        def lin(kw, kb):
            W = jax.random.uniform(kw, (D_MODEL, D_MODEL), minval=-s, maxval=s, dtype=jnp.float32)
            b = jax.random.uniform(kb, (D_MODEL,), minval=-s, maxval=s, dtype=jnp.float32)
            return (W, b)
        Wq, bq = lin(ks[2], ks[3])
        Wk, bk = lin(ks[4], ks[5])
        Wv, bv = lin(ks[6], ks[7])
        Wo, bo = lin(ks[8], ks[9])
        gamma = jnp.ones((D_MODEL,), dtype=jnp.float32)
        beta = jnp.zeros((D_MODEL,), dtype=jnp.float32)
        return {'x': x, 'adj': adj, 'Wq': Wq, 'bq': bq, 'Wk': Wk, 'bk': bk, 'Wv': Wv, 'bv': bv, 'Wo': Wo, 'bo': bo, 'gamma': gamma, 'beta': beta}
    _L0_gnn_all = _L0_gnn_setup()
    _L0_gnn_in = {k: v for k, v in _L0_gnn_all.items() if k in ('Wq', 'bq', 'Wk', 'bk', 'Wv', 'bv', 'Wo', 'bo', 'gamma', 'beta')}
    del _L0_gnn_all

    def _L1_gnn_setup():
        import jax, jax.numpy as jnp
        import numpy as np
        NUM_HEADS = 8
        EPS = 1e-09
        key = jax.random.key(seed)
        ks = jax.random.split(key, 8)
        B, N, D = (2, 1024, 256)
        s = 1.0 / np.sqrt(D)
        x = jax.random.normal(ks[0], (B, N, D), dtype=jnp.float32)
        adjacency = jax.random.uniform(ks[1], (B, N, N), dtype=jnp.float32)
        W_q = jax.random.normal(ks[2], (D, D), dtype=jnp.float32) * s
        W_k = jax.random.normal(ks[3], (D, D), dtype=jnp.float32) * s
        W_v = jax.random.normal(ks[4], (D, D), dtype=jnp.float32) * s
        b_q = jnp.zeros((D,), jnp.float32)
        b_k = jnp.zeros((D,), jnp.float32)
        b_v = jnp.zeros((D,), jnp.float32)
        w_g = jax.random.normal(ks[5], (2 * D,), dtype=jnp.float32) * (1.0 / np.sqrt(2 * D))
        b_g = jnp.zeros((), jnp.float32)
        return {'x': x, 'adjacency': adjacency, 'W_q': W_q, 'b_q': b_q, 'W_k': W_k, 'b_k': b_k, 'W_v': W_v, 'b_v': b_v, 'w_g': w_g, 'b_g': b_g}
    _L1_gnn_all = _L1_gnn_setup()
    _L1_gnn_in = {k: v for k, v in _L1_gnn_all.items() if k in ('W_q', 'b_q', 'W_k', 'b_k', 'W_v', 'b_v', 'w_g', 'b_g')}
    del _L1_gnn_all

    def _L2_gnn_setup():
        import jax, jax.numpy as jnp
        import numpy as np
        NUM_HID = 256
        BS, N = (8, 1024)
        NEG_BIG = -1000000000.0
        LEAKY_SLOPE = 0.01
        key = jax.random.key(seed)
        k_feats, k_adj, k_w, k_wq, k_wk = jax.random.split(key, 5)
        feats = jax.random.normal(k_feats, (BS, N, NUM_HID), dtype=jnp.float32)
        adj = (jax.random.uniform(k_adj, (BS, N, N)) < 0.05).astype(jnp.float32)
        eye = jnp.eye(N, dtype=jnp.float32)[None]
        adj_mat = jnp.maximum(adj, eye)
        s = 1.0 / np.sqrt(NUM_HID)
        W_fc = jax.random.uniform(k_w, (NUM_HID, NUM_HID), minval=-s, maxval=s, dtype=jnp.float32)
        b_fc = jnp.zeros((NUM_HID,), dtype=jnp.float32)
        w_q = jax.random.uniform(k_wq, (NUM_HID, 1), minval=-s, maxval=s, dtype=jnp.float32)
        b_q = jnp.zeros((1,), dtype=jnp.float32)
        w_k = jax.random.uniform(k_wk, (NUM_HID, 1), minval=-s, maxval=s, dtype=jnp.float32)
        b_k = jnp.zeros((1,), dtype=jnp.float32)
        return {'feats': feats, 'adj_mat': adj_mat, 'W_fc': W_fc, 'b_fc': b_fc, 'w_q': w_q, 'b_q': b_q, 'w_k': w_k, 'b_k': b_k}
    _L2_gnn_all = _L2_gnn_setup()
    _L2_gnn_in = {k: v for k, v in _L2_gnn_all.items() if k in ('W_fc', 'b_fc', 'w_q', 'b_q', 'w_k', 'b_k')}
    del _L2_gnn_all

    def _L3_gnn_setup():
        import jax, jax.numpy as jnp
        import numpy as np
        B, N, D, H = (8, 512, 256, 8)
        DK = D // H
        LN_EPS = 1e-05
        ADJ_MIN = 1e-08

        def _layer_norm(x, gamma, beta):
            mu = jnp.mean(x, axis=-1, keepdims=True)
            var = jnp.mean(jnp.square(x - mu), axis=-1, keepdims=True)
            return (x - mu) * jax.lax.rsqrt(var + LN_EPS) * gamma + beta
        key = jax.random.key(seed)
        ks = jax.random.split(key, 12)
        x = jax.random.normal(ks[0], (B, N, D), dtype=jnp.float32)
        adj = jax.random.uniform(ks[1], (B, N, N), dtype=jnp.float32)
        adj = adj / jnp.sum(adj, axis=-1, keepdims=True)
        s = 1.0 / np.sqrt(D)
        Wq = jax.random.normal(ks[2], (D, D), dtype=jnp.float32) * s
        bq = jnp.zeros((D,), dtype=jnp.float32)
        Wk = jax.random.normal(ks[3], (D, D), dtype=jnp.float32) * s
        bk = jnp.zeros((D,), dtype=jnp.float32)
        Wv = jax.random.normal(ks[4], (D, D), dtype=jnp.float32) * s
        bv = jnp.zeros((D,), dtype=jnp.float32)
        Wo = jax.random.normal(ks[5], (D, D), dtype=jnp.float32) * s
        bo = jnp.zeros((D,), dtype=jnp.float32)
        gamma = jnp.ones((D,), dtype=jnp.float32)
        beta = jnp.zeros((D,), dtype=jnp.float32)
        return {'x': x, 'adj': adj, 'Wq': Wq, 'bq': bq, 'Wk': Wk, 'bk': bk, 'Wv': Wv, 'bv': bv, 'Wo': Wo, 'bo': bo, 'gamma': gamma, 'beta': beta}
    _L3_gnn_all = _L3_gnn_setup()
    _L3_gnn_in = {k: v for k, v in _L3_gnn_all.items() if k in ('Wq', 'bq', 'Wk', 'bk', 'Wv', 'bv', 'Wo', 'bo', 'gamma', 'beta')}
    del _L3_gnn_all
    return {'x': x, 'adj': adj, 'L0_gnn_Wq': _L0_gnn_in['Wq'], 'L0_gnn_bq': _L0_gnn_in['bq'], 'L0_gnn_Wk': _L0_gnn_in['Wk'], 'L0_gnn_bk': _L0_gnn_in['bk'], 'L0_gnn_Wv': _L0_gnn_in['Wv'], 'L0_gnn_bv': _L0_gnn_in['bv'], 'L0_gnn_Wo': _L0_gnn_in['Wo'], 'L0_gnn_bo': _L0_gnn_in['bo'], 'L0_gnn_gamma': _L0_gnn_in['gamma'], 'L0_gnn_beta': _L0_gnn_in['beta'], 'L1_gnn_W_q': _L1_gnn_in['W_q'], 'L1_gnn_b_q': _L1_gnn_in['b_q'], 'L1_gnn_W_k': _L1_gnn_in['W_k'], 'L1_gnn_b_k': _L1_gnn_in['b_k'], 'L1_gnn_W_v': _L1_gnn_in['W_v'], 'L1_gnn_b_v': _L1_gnn_in['b_v'], 'L1_gnn_w_g': _L1_gnn_in['w_g'], 'L1_gnn_b_g': _L1_gnn_in['b_g'], 'L2_gnn_W_fc': _L2_gnn_in['W_fc'], 'L2_gnn_b_fc': _L2_gnn_in['b_fc'], 'L2_gnn_w_q': _L2_gnn_in['w_q'], 'L2_gnn_b_q': _L2_gnn_in['b_q'], 'L2_gnn_w_k': _L2_gnn_in['w_k'], 'L2_gnn_b_k': _L2_gnn_in['b_k'], 'L3_gnn_Wq': _L3_gnn_in['Wq'], 'L3_gnn_bq': _L3_gnn_in['bq'], 'L3_gnn_Wk': _L3_gnn_in['Wk'], 'L3_gnn_bk': _L3_gnn_in['bk'], 'L3_gnn_Wv': _L3_gnn_in['Wv'], 'L3_gnn_bv': _L3_gnn_in['bv'], 'L3_gnn_Wo': _L3_gnn_in['Wo'], 'L3_gnn_bo': _L3_gnn_in['bo'], 'L3_gnn_gamma': _L3_gnn_in['gamma'], 'L3_gnn_beta': _L3_gnn_in['beta']}

def reference(x, adj, L0_gnn_Wq, L0_gnn_bq, L0_gnn_Wk, L0_gnn_bk, L0_gnn_Wv, L0_gnn_bv, L0_gnn_Wo, L0_gnn_bo, L0_gnn_gamma, L0_gnn_beta, L1_gnn_W_q, L1_gnn_b_q, L1_gnn_W_k, L1_gnn_b_k, L1_gnn_W_v, L1_gnn_b_v, L1_gnn_w_g, L1_gnn_b_g, L2_gnn_W_fc, L2_gnn_b_fc, L2_gnn_w_q, L2_gnn_b_q, L2_gnn_w_k, L2_gnn_b_k, L3_gnn_Wq, L3_gnn_bq, L3_gnn_Wk, L3_gnn_bk, L3_gnn_Wv, L3_gnn_bv, L3_gnn_Wo, L3_gnn_bo, L3_gnn_gamma, L3_gnn_beta):
    import jax
    import jax.numpy as jnp

    def _L0_gnn_ref(x, adj, Wq, bq, Wk, bk, Wv, bv, Wo, bo, gamma, beta):
        import jax, jax.numpy as jnp
        import numpy as np
        D_MODEL = 256
        N_HEADS = 8
        D_HEAD = D_MODEL // N_HEADS
        B = 8
        N = 512
        EPS = 1e-05
        Bsz, n, _ = x.shape

        def proj(W, b):
            y = x @ W.T + b
            return y.reshape(Bsz, n, N_HEADS, D_HEAD).transpose(0, 2, 1, 3)
        q, k, v = (proj(Wq, bq), proj(Wk, bk), proj(Wv, bv))
        scores = jnp.einsum('bhqd,bhkd->bhqk', q, k) / np.sqrt(D_HEAD)
        mask = adj + jnp.eye(n, dtype=adj.dtype)[None] > 0
        scores = jnp.where(mask[:, None], scores, -jnp.inf)
        attn = jax.nn.softmax(scores, axis=-1)
        out = jnp.einsum('bhqk,bhkd->bhqd', attn, v)
        out = out.transpose(0, 2, 1, 3).reshape(Bsz, n, D_MODEL)
        out = out @ Wo.T + bo
        h = x + out
        mu = jnp.mean(h, axis=-1, keepdims=True)
        var = jnp.mean(jnp.square(h - mu), axis=-1, keepdims=True)
        return (h - mu) * jax.lax.rsqrt(var + EPS) * gamma + beta

    def _L1_gnn_ref(x, adjacency, W_q, b_q, W_k, b_k, W_v, b_v, w_g, b_g):
        import jax, jax.numpy as jnp
        import numpy as np
        NUM_HEADS = 8
        EPS = 1e-09
        B, N, D = x.shape
        H = NUM_HEADS
        hd = D // H
        Q = (x @ W_q + b_q).reshape(B, N, H, hd)
        K = (x @ W_k + b_k).reshape(B, N, H, hd)
        V = (x @ W_v + b_v).reshape(B, N, H, hd)
        scores = jnp.einsum('bihd,bjhd->bhij', Q, K) / jnp.sqrt(jnp.float32(hd))
        a = x @ w_g[:D]
        c = x @ w_g[D:]
        soul_bias = a[:, :, None] + c[:, None, :] + b_g
        scores = scores + (soul_bias + jnp.log(adjacency + EPS))[:, None, :, :]
        attn = jax.nn.softmax(scores, axis=-1)
        out = jnp.einsum('bhij,bjhd->bihd', attn, V).reshape(B, N, D)
        return out + x

    def _L2_gnn_ref(feats, adj_mat, W_fc, b_fc, w_q, b_q, w_k, b_k):
        import jax, jax.numpy as jnp
        import numpy as np
        NUM_HID = 256
        BS, N = (8, 1024)
        NEG_BIG = -1000000000.0
        LEAKY_SLOPE = 0.01
        feat_proj = jnp.einsum('bnd,de->bne', feats, W_fc) + b_fc
        q = jnp.einsum('bnd,do->bno', feat_proj, w_q) + b_q
        k = jnp.einsum('bnd,do->bno', feat_proj, w_k) + b_k
        logits = q + jnp.swapaxes(k, 2, 1)
        masked = logits + (1.0 - adj_mat) * NEG_BIG
        masked = jnp.where(masked >= 0, masked, LEAKY_SLOPE * masked)
        atten = jax.nn.softmax(masked, axis=-1)
        out = jnp.einsum('bnm,bmd->bnd', atten, feat_proj)
        return out + feats

    def _L3_gnn_ref(x, adj, Wq, bq, Wk, bk, Wv, bv, Wo, bo, gamma, beta):
        import jax, jax.numpy as jnp
        import numpy as np
        B, N, D, H = (8, 512, 256, 8)
        DK = D // H
        LN_EPS = 1e-05
        ADJ_MIN = 1e-08

        def _layer_norm(x, gamma, beta):
            mu = jnp.mean(x, axis=-1, keepdims=True)
            var = jnp.mean(jnp.square(x - mu), axis=-1, keepdims=True)
            return (x - mu) * jax.lax.rsqrt(var + LN_EPS) * gamma + beta
        b, n, d = x.shape
        q = (x @ Wq.T + bq).reshape(b, n, H, DK).transpose(0, 2, 1, 3)
        k = (x @ Wk.T + bk).reshape(b, n, H, DK).transpose(0, 2, 1, 3)
        v = (x @ Wv.T + bv).reshape(b, n, H, DK).transpose(0, 2, 1, 3)
        logits = jnp.einsum('bhqd,bhkd->bhqk', q, k) / np.sqrt(DK)
        logits = logits + jnp.log(jnp.clip(adj, ADJ_MIN, None))[:, None, :, :]
        attn = jax.nn.softmax(logits, axis=-1)
        out = jnp.einsum('bhqk,bhkd->bhqd', attn, v)
        out = out.transpose(0, 2, 1, 3).reshape(b, n, d)
        out = out @ Wo.T + bo
        return _layer_norm(x + out, gamma, beta)
    x = _L0_gnn_ref(x, adj, L0_gnn_Wq, L0_gnn_bq, L0_gnn_Wk, L0_gnn_bk, L0_gnn_Wv, L0_gnn_bv, L0_gnn_Wo, L0_gnn_bo, L0_gnn_gamma, L0_gnn_beta)
    x = _L1_gnn_ref(x, adj, L1_gnn_W_q, L1_gnn_b_q, L1_gnn_W_k, L1_gnn_b_k, L1_gnn_W_v, L1_gnn_b_v, L1_gnn_w_g, L1_gnn_b_g)
    x = _L2_gnn_ref(x, adj, L2_gnn_W_fc, L2_gnn_b_fc, L2_gnn_w_q, L2_gnn_b_q, L2_gnn_w_k, L2_gnn_b_k)
    x = _L3_gnn_ref(x, adj, L3_gnn_Wq, L3_gnn_bq, L3_gnn_Wk, L3_gnn_bk, L3_gnn_Wv, L3_gnn_bv, L3_gnn_Wo, L3_gnn_bo, L3_gnn_gamma, L3_gnn_beta)
    return x

_drawn_inputs = setup_inputs


def setup_inputs(seed=0):
    import zlib

    import numpy as np

    out = dict(_drawn_inputs(seed))
    spreads = {'L0_gnn_gamma': (1.0, 0.2),
     'L0_gnn_beta': (0.0, 0.1),
     'L1_gnn_b_q': (0.0, 0.1),
     'L1_gnn_b_k': (0.0, 0.8),
     'L1_gnn_b_v': (0.0, 0.1),
     'L2_gnn_b_fc': (0.0, 0.1),
     'L3_gnn_bq': (0.0, 0.1),
     'L3_gnn_bk': (0.0, 0.8),
     'L3_gnn_bv': (0.0, 0.1),
     'L3_gnn_bo': (0.0, 0.1),
     'L3_gnn_gamma': (1.0, 0.2),
     'L3_gnn_beta': (0.0, 0.1)}
    factors = {'L0_gnn_bq': 8.0, 'L0_gnn_bk': 8.0}
    for name, (base, spread) in spreads.items():
        noise = np.random.default_rng([zlib.crc32(name.encode()), seed]).standard_normal(out[name].shape)
        drawn = base * np.exp(spread * noise) if base else spread * noise
        out[name] = jnp.asarray(drawn.astype(out[name].dtype))
    for name, factor in factors.items():
        out[name] = (out[name] * factor).astype(out[name].dtype)
    return out
```

```python
from contextlib import ExitStack

import concourse.bass as bass
from concourse import mybir

F32 = mybir.dt.float32
F32R = mybir.dt.float32r
BF16 = mybir.dt.bfloat16
ALU = mybir.AluOpType
ACT = mybir.ActivationFunctionType
AX_X = mybir.AxisListType.X

P = 128
LANES = 2
LAYERS = 4
START = 1
MHA = {0: 0, 1: 1, 3: 2}
LN = {0: 0, 3: 1}
LN_EPS = 1e-5
LOG_EPS = 1e-9
ADJ_MIN = 1e-8
MASKED = -1e30
NEG_BIG = -1e9
SLOPE = 0.01

K_LO, K_HI, Q_HI, Q_LO = range(4)
ROW_EXTRA = 96



def schedule():
    def head(l):
        return ["T", "Q", "V", "S"] if l in MHA else ["T", "G", "K"]

    def tail(l):
        return ["M", "E", "O", "F"] if l in MHA else ["W", "A"]

    order = []
    for l in range(LAYERS):
        a_head, a_tail = [(s, 0, l) for s in head(l)], [(s, 0, l) for s in tail(l)]
        b_head = [(s, 1, l) for s in head(l)]
        b_tail = [(s, 1, l - 1) for s in tail(l - 1)] if l else []
        order += a_head[:2] + b_tail[:1] + a_head[2:3] + b_tail[1:] + a_head[3:]
        order += b_head[:2] + a_tail[:1] + b_head[2:3] + a_tail[1:] + b_head[3:]
    order += [(s, 1, LAYERS - 1) for s in tail(LAYERS - 1)]
    return order


ORDER = schedule()

USES = {"T": [("ga", "x")], "Q": [("gb", "q"), ("ga", "k")], "V": [("gb", "v")],
        "S": [("sc0", "s0"), ("sc1", "s1"), ("sc0", "s2"), ("sc1", "s3")],
        "M": [("gb", "m")],
        "E": [("sc0", "e0"), ("sc1", "e1"), ("sc0", "e2"), ("sc1", "e3")],
        "O": [("den", "d"), ("att", "o")], "F": [("ga", "f")],
        "G": [("ga", "fp0"), ("gb", "fp1")], "K": [("ga", "kb")],
        "W": [("gb", "pt")], "A": [("ga", "av")]}


def uses_of(stage, layer):
    return USES[stage] + ([("gb", "ca")] if (stage, layer) == ("Q", 1) else [])


AREAS = ("ga", "gb", "att", "den", "sc0", "sc1")
USE_INDEX = {a: {} for a in AREAS}
for _stage, _lane, _layer in ORDER:
    for _area, _what in uses_of(_stage, _layer):
        USE_INDEX[_area][(_what, _lane, _layer)] = len(USE_INDEX[_area])


def gnn_stack(nc, x, adj, adj_t, w, out):
    B, N, D = x.shape
    H, DH = 8, D // 8
    T = N // P
    C = D // P
    G = P // DH
    STEPS = B // LANES
    SCALE = 1.0 / float(DH) ** 0.5
    CHUNK = G * N
    assert N == 2 * P and D == 2 * P

    with ExitStack() as ctx:
        def sb(name, shape, dt=F32):
            return ctx.enter_context(nc.sbuf_tensor(name, shape, dt))

        def sem(name):
            return ctx.enter_context(nc.semaphore(name))

        counted = []

        def lane_sems(name):
            sems = [sem(f"{name}{n}") for n in range(LANES)]
            counted.extend(sems)
            return sems

        def lane_sb(name, shape, dt=F32):
            return [sb(f"{name}{n}", shape, dt) for n in range(LANES)]

        area = {a: ctx.enter_context(nc.psum_tensor(a, [P, CHUNK if a[:2] == "sc" else 512], F32)) for a in AREAS}

        names = ["q0", "k0", "v0", "q1", "k1", "v1", "q3", "k3", "v3", "fc"]
        raw = sb("raw", [P, 2, C, D])
        w_hi = {n: sb(f"wh_{n}", [P, C, D + 2 * (n == "fc")], F32R) for n in names}
        w_lo = {n: sb(f"wl_{n}", [P, C, D + 2 * (n == "fc")], F32R) for n in names}
        w_o = {l: sb(f"wo{l}", [P, C, D]) for l in LN}
        w_ca = sb("w_ca", [P, C, 2])
        b_col = {n: sb(f"bc_{n}", [P, C]) for n in ("q0", "k0", "q1", "k1", "q3", "k3")}
        b_row = {n: sb(f"br_{n}", [P, D]) for n in ("v0", "v1", "v3", "o0", "o3", "g0", "g3", "e0", "e3")}
        fc_row = sb("fc_row", [P, D + 2])
        fc_ext = sb("fc_ext", [P, C, D + 2])
        w_qk2 = sb("w_qk2", [P, 2, D])
        b_qk2 = sb("b_qk2", [P, 2])
        junk = sb("junk", [P, D])
        bg_col = sb("bg_col", [2, 1])
        eps_col = sb("eps_col", [P, 1])
        log_eps_col = sb("log_eps_col", [P, 1])
        ident = sb("ident", [P, P])
        ident_b = sb("ident_b", [P, P], BF16)
        eye = sb("eye", [P, T, N])
        ones = sb("ones", [P, P])

        x_in = lane_sb("x_in", [P, T, D])
        xs = lane_sb("xs", [P, T, D])
        xb = lane_sb("xb", [P, T, D])
        xt_hi = lane_sb("xt_hi", [P, C, N], F32R)
        xt_lo = lane_sb("xt_lo", [P, C, N], F32R)
        stack = lane_sb("stack", [P, C, 2, G, N], F32R)
        v_sb = lane_sb("v_sb", [P, T, D])
        probs = lane_sb("probs", [P, T, H, N])
        negm = lane_sb("negm", [P, H, T])
        m_hl = lane_sb("m_hl", [H * T, 2, P], F32R)
        ca_hl = lane_sb("ca_hl", [2, 2, N], F32R)
        rden = lane_sb("rden", [P, C, N])
        o_t = lane_sb("o_t", [P, C, N])
        h_sb = lane_sb("h_sb", [P, T, D])
        bn6 = lane_sb("bn6", [P, T, 6])
        mv = lane_sb("mv", [P, T, 2])
        std = lane_sb("std", [P, T])
        rstd = lane_sb("rstd", [P, T])
        adj_r = lane_sb("adj_r", [P, T, N])
        adj_c = lane_sb("adj_c", [P, T, N])
        mask_r = lane_sb("mask_r", [P, T, N], BF16)
        mask_c = lane_sb("mask_c", [P, T, N], BF16)
        wt1 = lane_sb("wt1", [P, T, N])
        wt3 = lane_sb("wt3", [P, T, N])
        nb2 = lane_sb("nb2", [P, T, N])
        flat = [probs[n][:, :, :, :].rearrange("p t h n -> p (t h n)") for n in range(LANES)]
        qk = [flat[n][:, 0:4 * C * N].bitcast(F32R).rearrange("p (c s n) -> p c s n", s=4, c=C) for n in range(LANES)]
        fp = lane_sb("fp", [P, T, D + 2])
        dk = [flat[n][:, 0:T * P].rearrange("p (t n) -> p t n", t=T) for n in range(LANES)]
        lg = [flat[n][:, 512:1024].rearrange("p (t n) -> p t n", t=T) for n in range(LANES)]
        lk = [flat[n][:, 1024:1536].rearrange("p (t n) -> p t n", t=T) for n in range(LANES)]
        p2 = [flat[n][:, 1536:2048].rearrange("p (t n) -> p t n", t=T) for n in range(LANES)]
        p2t = [flat[n][:, 2048:2560].rearrange("p (t n) -> p t n", t=T) for n in range(LANES)]
        m2 = lane_sb("m2", [P, T])
        s2 = lane_sb("s2", [P, T])
        r2 = lane_sb("r2", [P, T])

        w_loaded, w_split = sem("w_loaded"), sem("w_split")
        w_raw = [sem("w_raw0"), sem("w_raw1")]
        consts_set, fc_set = sem("consts_set"), sem("fc_set")
        full = {a: sem(f"{a}_full") for a in AREAS}
        x_loaded, adj_loaded = lane_sems("x_loaded"), lane_sems("adj_loaded")
        prepared, xb_set = lane_sems("prepared"), lane_sems("xb_set")
        x_set = lane_sems("x_set")
        xt_hi_set, xt_lo_set = lane_sems("xt_hi_set"), lane_sems("xt_lo_set")
        qk_hi_set, qk_lo_set = lane_sems("qk_hi_set"), lane_sems("qk_lo_set")
        ca_hi_set, ca_lo_set, ca_rows = lane_sems("ca_hi_set"), lane_sems("ca_lo_set"), lane_sems("ca_rows")
        stacked = lane_sems("stacked")
        v_set, maxed = lane_sems("v_set"), lane_sems("maxed")
        m_hi_set, m_lo_set, m_rows = lane_sems("m_hi_set"), lane_sems("m_lo_set"), lane_sems("m_rows")
        exped, weighted = lane_sems("exped"), lane_sems("weighted")
        rden_set, o_set = lane_sems("rden_set"), lane_sems("o_set")
        ln_done, std_set = lane_sems("ln_done"), lane_sems("std_set")
        fp_set, dk_set, l2_done = lane_sems("fp_set"), lane_sems("dk_set"), lane_sems("l2_done")
        p2_set, p2t_set = lane_sems("p2_set"), lane_sems("p2t_set")
        stored = lane_sems("stored")
        waits_passed = sem("waits_passed")

        def per_step(it, each, n):
            return START + it * each + n

        def per_layer(it, l, each=1):
            return START + it * (LAYERS * each) + l * each

        def per_mha(it, l, each=1):
            return START + it * (len(MHA) * each) + MHA[l] * each

        def per_ln(it, l, each=1):
            return START + it * (len(LN) * each) + LN[l] * each

        def use(it, a, what, lane, l):
            return it * len(USE_INDEX[a]) + USE_INDEX[a][(what, lane, l)]

        def own_slot(eng):
            eng.sem_inc(waits_passed, 1)

        def filled(eng, it, a, what, lane, l):
            eng.wait_ge(full[a], use(it, a, what, lane, l) + 1)

        def reader(what, n, l):
            mha, layer = MHA.get(l, 0), l + 1
            if what[0] in "se":
                done = {"s": maxed, "e": exped}[what[0]][n]
                return done, len(MHA) * 2 * T, mha * 2 * T + int(what[1]) + 1
            if what == "f" and l in LN:
                return ln_done[n], len(LN) * 8, LN[l] * 8 + 1
            if what[:2] == "fp":
                return fp_set[n], T, int(what[2]) + 1
            return {"x": (xt_lo_set[n], LAYERS, layer), "f": (x_set[n], LAYERS, layer), "av": (x_set[n], LAYERS, layer),
                    "q": (qk_lo_set[n], len(MHA) * 2 * C, mha * 2 * C + C),
                    "k": (qk_lo_set[n], len(MHA) * 2 * C, mha * 2 * C + 2 * C),
                    "v": (v_set[n], len(MHA), mha + 1), "m": (m_lo_set[n], len(MHA), mha + 1),
                    "d": (rden_set[n], len(MHA), mha + 1), "o": (o_set[n], len(MHA), mha + 1),
                    "ca": (ca_lo_set[n], 1, 1), "kb": (l2_done[n], 5, 2), "pt": (p2t_set[n], 1, 1)}[what]

        def emptied(eng, it, a, what, lane, l):
            order = list(USE_INDEX[a])
            i = USE_INDEX[a][(what, lane, l)]
            done, each, value = reader(*order[i - 1])
            eng.wait_ge(done, per_step(it, each, value if i else 0))

        def terms(hi_a, lo_a, hi_b, lo_b):
            return ((hi_a, hi_b), (hi_a, lo_b), (lo_a, hi_b))

        x_steps = x.rearrange("(s l) (t p) d -> s l p t d", l=LANES, p=P)
        adj_steps = adj.rearrange("(s l) (t p) j -> s l p t j", l=LANES, p=P)
        adj_t_steps = adj_t.rearrange("(s l) (t p) i -> s l p t i", l=LANES, p=P)
        out_steps = out.rearrange("(s l) (t p) d -> s l p t d", l=LANES, p=P)

        plain = [(w_o[l][:], w[f"o{l}"].rearrange("(c p) e -> p c e", p=P)) for l in LN]
        plain += [(w_ca[:], w["g1"].rearrange("p (c k) -> p c k", c=C))]
        plain += [(b_col[n][:], w[f"b{n}"]) for n in b_col]
        plain += [(b_row[n][:], w[f"b{n}"].to_broadcast([P, D])) for n in b_row]
        plain += [(fc_row[:, 0:D], w["bfc"].to_broadcast([P, D]))]
        plain += [(w_qk2[:, j, :], w[n].to_broadcast([P, D])) for j, n in enumerate(("wq2", "wk2"))]
        plain += [(b_qk2[:, j:j + 1], w[n].to_broadcast([P, 1])) for j, n in enumerate(("bq2", "bk2"))]
        plain += [(bg_col[:], w["bg"])]
        plain += [(fc_ext[:, :, 0:D], w["fc"].rearrange("(c p) e -> p c e", p=P))]
        FC_STEPS = 2 * C + 2 + 1
        SPLIT_EACH = 3
        CONSTS = 13
        STACK_DMAS = 4 * G

        block = ctx.enter_context(nc.Block())

        @block.sync
        def _(sp):
            for s in counted:
                sp.sem_inc(s, START)
            for dst, src in plain:
                sp.dma_start(dst, src).then_inc(w_loaded, 16)
            for n, name in enumerate(names[:-1]):
                if n >= 2:
                    sp.wait_ge(w_split, SPLIT_EACH * (n - 1))
                sp.dma_start(raw[:, n % 2], w[name].rearrange("(c p) e -> p c e", p=P)).then_inc(w_raw[n % 2], 16)
            sp.wait_ge(consts_set, CONSTS)

            with sp.Fori(0, STEPS) as it:
                for n in range(LANES):
                    if True:
                        sp.wait_ge(xt_hi_set[n], per_layer(it, 0))
                        own_slot(sp)
                        sp.wait_ge(xb_set[n], per_ln(it, 0))
                        own_slot(sp)
                        sp.dma_start(x_in[n][:], x_steps[it, n]).then_inc(x_loaded[n], 16)
                        sp.wait_ge(prepared[n], per_step(it, 5, 0))
                        own_slot(sp)
                        sp.dma_start(adj_r[n][:], adj_steps[it, n]).then_inc(adj_loaded[n], 16)
                        sp.dma_start(adj_c[n][:], adj_t_steps[it, n]).then_inc(adj_loaded[n], 16)
                for s, n, l in ORDER:
                    if s == "Q":
                        sp.wait_ge(qk_hi_set[n], per_mha(it, l, 2 * C) + 2 * C)
                        for side, slot in ((0, K_HI), (1, Q_HI)):
                            for g in range(G):
                                sp.dma_start(stack[n][0:DH, :, side, g, :].bitcast(F32),
                                             qk[n][DH * g:DH * (g + 1), :, slot, :].bitcast(F32)).then_inc(stacked[n], 16)
                        sp.wait_ge(qk_lo_set[n], per_mha(it, l, 2 * C) + 2 * C)
                        for block_row, k_slot in ((1, K_LO), (2, K_HI)):
                            for g in range(G):
                                sp.dma_start(stack[n][DH * block_row:DH * (block_row + 1), :, :, g, :].bitcast(F32),
                                             qk[n][DH * g:DH * (g + 1), :, k_slot::2, :].bitcast(F32))\
                                    .then_inc(stacked[n], 16)
                        if l == 1:
                            sp.wait_ge(ca_hi_set[n], per_step(it, 1, 1))
                            own_slot(sp)
                            sp.wait_ge(ca_lo_set[n], per_step(it, 1, 1))
                            for row, side in ((0, 1), (2, 0)):
                                for part in range(2):
                                    src = ca_hl[n][1 - side:2 - side, part, :].unsqueeze(1).to_broadcast([1, G, N])
                                    for c in range(C):
                                        dst = stack[n][ROW_EXTRA + row + part:ROW_EXTRA + row + part + 1, c, side, :, :]
                                        sp.dma_start(dst.bitcast(F32), src.bitcast(F32)).then_inc(ca_rows[n], 16)
                    elif s == "M":
                        sp.wait_ge(m_hi_set[n], per_mha(it, l) + 1)
                        own_slot(sp)
                        sp.wait_ge(m_lo_set[n], per_mha(it, l) + 1)
                        first = ROW_EXTRA + (4 if l == 1 else 0)
                        for part in range(2):
                            for c in range(C):
                                dst = stack[n][first + part:first + part + 1, c, 1, :, :]
                                sp.dma_start(dst.rearrange("o g (t p) -> o (g t) p", t=T).bitcast(F32),
                                             m_hl[n][G * T * c:G * T * (c + 1), part, :].bitcast(F32))\
                                    .then_inc(m_rows[n], 16)
                    elif s == "F" and l == LAYERS - 1:
                        sp.wait_ge(x_set[n], per_layer(it, l) + 1)
                        own_slot(sp)
                        sp.dma_start(out_steps[it, n], xs[n][:]).then_inc(stored[n], 16)
            for n in range(LANES):
                sp.wait_ge(stored[n], START + 16 * STEPS)

        @block.gpsimd
        def _(pool):
            pool.memset(ident[:], 0.0).then_inc(consts_set, 1)
            pool.memset(eye[:], 0.0).then_inc(consts_set, 1)
            pool.memset(ones[:], 1.0).then_inc(consts_set, 1)
            pool.memset(eps_col[:], LN_EPS).then_inc(consts_set, 1)
            pool.memset(log_eps_col[:], LOG_EPS).then_inc(consts_set, 1)
            pool.wait_ge(consts_set, 5)
            pool.affine_select(out=ident[:], in_=ident[:], compare_op=ALU.not_equal, fill=1.0, base=0,
                               pattern=[[-1, P]], channel_multiplier=1).then_inc(consts_set, 1)
            pool.affine_select(out=eye[:], in_=eye[:], compare_op=ALU.not_equal, fill=1.0, base=0,
                               pattern=[[P, T], [-1, N]], channel_multiplier=1).then_inc(consts_set, 1)
            pool.wait_ge(consts_set, 7)
            pool.tensor_copy(ident_b[:], ident[:]).then_inc(consts_set, 1)
            pool.wait_ge(consts_set, 8)
            for n in range(LANES):
                pool.memset(stack[n][ROW_EXTRA:P].bitcast(F32), 1.0).then_inc(consts_set, 1)
                pool.wait_ge(consts_set, 9 + n)
            pool.wait_ge(w_loaded, 16 * len(plain))
            for name in ("q0", "q1", "q3"):
                pool.tensor_scalar(b_col[name][:], b_col[name][:], SCALE, None, ALU.mult).then_inc(consts_set, 1)
            pool.wait_ge(consts_set, CONSTS)

            with pool.Fori(0, STEPS) as it:
                for n in range(LANES):
                    first = per_step(it, 5, 0)
                    pool.wait_ge(adj_loaded[n], per_step(it, 32, 32))
                    pool.tensor_tensor(wt1[n][:], adj_r[n][:], eye[:], ALU.add).then_inc(prepared[n], 1)
                    pool.tensor_tensor(wt3[n][:], adj_c[n][:], eye[:], ALU.add).then_inc(prepared[n], 1)
                    pool.wait_ge(prepared[n], first + 2)
                    pool.tensor_tensor(nb2[n][:], ones[:, 0:1].unsqueeze(1).to_broadcast([P, T, N]), adj_r[n][:],
                                       ALU.subtract)
                    pool.tensor_scalar(mask_r[n][:], wt1[n][:], 0.0, MASKED, ALU.is_le, ALU.mult).then_inc(prepared[n], 1)
                    pool.tensor_scalar(mask_c[n][:], wt3[n][:], 0.0, MASKED, ALU.is_le, ALU.mult).then_inc(prepared[n], 1)
                    pool.wait_ge(prepared[n], first + 4)
                    pool.tensor_tensor(wt1[n][:], adj_c[n][:], log_eps_col[:].unsqueeze(1).to_broadcast([P, T, N]), ALU.add)
                    pool.tensor_scalar(wt3[n][:], adj_c[n][:], ADJ_MIN, None, ALU.max).then_inc(prepared[n], 1)
                for s, n, l in ORDER:
                    if s == "T" and l in LN:
                        src = x_in[n] if l == 0 else xs[n]
                        if l == 0:
                            pool.wait_ge(x_loaded[n], per_step(it, 16, 16))
                        else:
                            pool.wait_ge(x_set[n], per_layer(it, l))
                        bias = b_row[f"o{l}"][:].unsqueeze(1).to_broadcast([P, T, D])
                        pool.tensor_tensor(xb[n][:], src[:], bias, ALU.add).then_inc(xb_set[n], 1)
                    elif s == "E" and l > 0:
                        wt = wt1 if l == 1 else wt3
                        pool.wait_ge(prepared[n], per_step(it, 5, 5))
                        for c in range(2 * T):
                            t, grp = c % T, c // T
                            pool.wait_ge(exped[n], per_mha(it, l, 2 * T) + c + 1)
                            part = probs[n][:, t, G * grp:G * (grp + 1), :]
                            pool.tensor_tensor(part, part, wt[n][:, t, :].unsqueeze(1).to_broadcast([P, G, N]), ALU.mult)\
                                .then_inc(weighted[n], 1)

        @block.tensor
        def _(pe):
            pe.wait_ge(consts_set, CONSTS)
            pe.wait_ge(w_loaded, 16 * len(plain))
            pe.wait_ge(w_split, SPLIT_EACH * len(names))

            def project(a, dst, stat, mov, cols):
                for c in range(C):
                    for i, (st, mv_) in enumerate(terms(stat[0], stat[1], mov[0], mov[1])):
                        mm = pe.matmul(dst, st(c), mv_(c), start=(c == 0 and i == 0), stop=(c == C - 1 and i == 2))
                return mm

            with pe.Fori(0, STEPS) as it:
                for s, n, l in ORDER:
                    key = (n, l)
                    xh, xl = xt_hi[n], xt_lo[n]
                    if s == "T":
                        if l == 0:
                            pe.wait_ge(x_loaded[n], per_step(it, 16, 16))
                        else:
                            pe.wait_ge(x_set[n], per_layer(it, l))
                        src = x_in[n] if l == 0 else xs[n]
                        emptied(pe, it, "ga", "x", *key)
                        for c in range(C):
                            for t in range(T):
                                mm = pe.transpose(area["ga"][:, c * N + t * P:c * N + (t + 1) * P],
                                                  src[:, t, c * P:(c + 1) * P], ident[:])
                        mm.then_inc(full["ga"], 1)
                    elif s == "Q":
                        pe.wait_ge(xt_lo_set[n], per_layer(it, l) + 1)
                        pe.wait_ge(xt_hi_set[n], per_layer(it, l) + 1)
                        for a, what in (("gb", "q"), ("ga", "k")):
                            emptied(pe, it, a, what, *key)
                            wh, wl = w_hi[f"{what}{l}"], w_lo[f"{what}{l}"]
                            for m in range(C):
                                mm = project(a, area[a][:, m * N:(m + 1) * N],
                                             [lambda c, m=m: wh[:, c, m * P:(m + 1) * P],
                                              lambda c, m=m: wl[:, c, m * P:(m + 1) * P]],
                                             [lambda c: xh[:, c, :], lambda c: xl[:, c, :]], N)
                            mm.then_inc(full[a], 1)
                        if l == 1:
                            emptied(pe, it, "gb", "ca", *key)
                            i = 0
                            for c in range(C):
                                for part in (xh, xl):
                                    mm = pe.matmul(area["gb"][0:2, 0:N], w_ca[:, c, :], part[:, c, :].bitcast(F32),
                                                   start=(i == 0), stop=(i == 2 * C - 1))
                                    i += 1
                            mm.then_inc(full["gb"], 1)
                    elif s == "V":
                        emptied(pe, it, "gb", "v", *key)
                        wh, wl = w_hi[f"v{l}"], w_lo[f"v{l}"]
                        for t in range(T):
                            mm = project("gb", area["gb"][:, t * D:(t + 1) * D],
                                         [lambda c, t=t: xh[:, c, t * P:(t + 1) * P],
                                          lambda c, t=t: xl[:, c, t * P:(t + 1) * P]],
                                         [lambda c: wh[:, c, :], lambda c: wl[:, c, :]], D)
                        mm.then_inc(full["gb"], 1)
                    elif s in "SE":
                        if s == "S":
                            pe.wait_ge(stacked[n], per_mha(it, l, STACK_DMAS * 16) + STACK_DMAS * 16)
                            if l == 1:
                                pe.wait_ge(ca_rows[n], per_step(it, 128, 128))
                            if l == 0:
                                pe.wait_ge(prepared[n], per_step(it, 5, 4))
                            rows = ROW_EXTRA + (4 if l == 1 else 0)
                            st, mo = 1, 0
                        else:
                            pe.wait_ge(m_rows[n], per_mha(it, l, 2 * C * 16) + 2 * C * 16)
                            rows = ROW_EXTRA + (6 if l == 1 else 2)
                            st, mo = 0, 1
                        for c in range(2 * T):
                            t, grp = c % T, c // T
                            a = f"sc{c % 2}"
                            emptied(pe, it, a, f"{s.lower()}{c}", *key)
                            for j in range(G):
                                masked = l == 0
                                if masked and j % 2 == 0:
                                    pe.matmul(area[a][:, j * N:(j + 2) * N], ident_b[:],
                                              (mask_r if s == "S" else mask_c)[n][:, t, :].unsqueeze(1).to_broadcast([P, 2, N]),
                                              start=True, stop=False, skip_group_check=True)
                                mm = pe.matmul(area[a][:, j * N:(j + 1) * N],
                                               stack[n][0:rows, grp, st, j, t * P:(t + 1) * P],
                                               stack[n][0:rows, grp, mo, j, :],
                                               start=not masked, stop=True, skip_group_check=masked)
                            mm.then_inc(full[a], 1)
                    elif s == "M":
                        pe.wait_ge(maxed[n], per_mha(it, l, 2 * T) + 2 * T)
                        emptied(pe, it, "gb", "m", *key)
                        pe.transpose(area["gb"][0:H * T, 0:P], negm[n][:, :, :].rearrange("p h t -> p (h t)"),
                                     ident[:]).then_inc(full["gb"], 1)
                    elif s == "O":
                        pe.wait_ge(v_set[n], per_mha(it, l) + 1)
                        emptied(pe, it, "den", "d", *key)
                        emptied(pe, it, "att", "o", *key)
                        for grp in range(C):
                            for t in range(T):
                                chunk = T * grp + t + 1
                                if l == 0:
                                    pe.wait_ge(exped[n], per_mha(it, l, 2 * T) + chunk)
                                else:
                                    pe.wait_ge(weighted[n], per_step(it, 4 * T, (MHA[l] - 1) * 2 * T + chunk))
                                for a, stat in (("den", None), ("att", v_sb[n])):
                                    for g in range(G):
                                        head = G * grp + g
                                        lhs = ones[:, 0:DH] if stat is None else stat[:, t, head * DH:(head + 1) * DH]
                                        mm = pe.matmul(area[a][DH * g:DH * (g + 1), grp * N:(grp + 1) * N], lhs,
                                                       probs[n][:, t, head, :], start=(t == 0), stop=(t == T - 1))
                                    if grp == C - 1 and t == T - 1:
                                        mm.then_inc(full[a], 1)
                    elif s == "F":
                        pe.wait_ge(o_set[n], per_mha(it, l) + 1)
                        emptied(pe, it, "ga", "f", *key)
                        for t in range(T):
                            for c in range(C):
                                if l in LN:
                                    mm = pe.matmul(area["ga"][:, t * D:(t + 1) * D], o_t[n][:, c, t * P:(t + 1) * P],
                                                   w_o[l][:, c, :], start=(c == 0), stop=(c == C - 1))
                                else:
                                    mm = pe.transpose(area["ga"][:, t * D + c * P:t * D + (c + 1) * P],
                                                      o_t[n][:, c, t * P:(t + 1) * P], ident[:])
                        mm.then_inc(full["ga"], 1)
                    elif s == "G":
                        pe.wait_ge(xt_lo_set[n], per_layer(it, l) + 1)
                        pe.wait_ge(xt_hi_set[n], per_layer(it, l) + 1)
                        for t, a in enumerate(("ga", "gb")):
                            emptied(pe, it, a, f"fp{t}", *key)
                            project(a, area[a][:, 0:D + 2],
                                    [lambda c, t=t: xh[:, c, t * P:(t + 1) * P],
                                     lambda c, t=t: xl[:, c, t * P:(t + 1) * P]],
                                    [lambda c: w_hi["fc"][:, c, :], lambda c: w_lo["fc"][:, c, :]], D + 2)\
                                .then_inc(full[a], 1)
                    elif s == "K":
                        pe.wait_ge(dk_set[n], per_step(it, T, T))
                        emptied(pe, it, "ga", "kb", *key)
                        for t in range(T):
                            mm = pe.matmul(area["ga"][:, t * P:(t + 1) * P], ones[:], dk[n][:, t, :],
                                           start=True, stop=True)
                        mm.then_inc(full["ga"], 1)
                    elif s == "W":
                        pe.wait_ge(p2_set[n], per_step(it, T, T))
                        emptied(pe, it, "gb", "pt", *key)
                        for j in range(T):
                            for t in range(T):
                                mm = pe.transpose(area["gb"][:, j * N + t * P:j * N + (t + 1) * P],
                                                  p2[n][:, t, j * P:(j + 1) * P], ident[:])
                        mm.then_inc(full["gb"], 1)
                    elif s == "A":
                        pe.wait_ge(p2t_set[n], per_step(it, 1, 1))
                        emptied(pe, it, "ga", "av", *key)
                        for t in range(T):
                            for j in range(T):
                                mm = pe.matmul(area["ga"][:, t * D:(t + 1) * D], p2t[n][:, j, t * P:(t + 1) * P],
                                               fp[n][:, j, 0:D], start=(j == 0), stop=(j == T - 1))
                        mm.then_inc(full["ga"], 1)

        @block.scalar
        def _(act):
            act.wait_ge(consts_set, CONSTS)
            with act.Fori(0, STEPS) as it:
                for s, n, l in ORDER:
                    key = (n, l)
                    if s == "T":
                        filled(act, it, "ga", "x", *key)
                        act.activation(xt_hi[n][:].rearrange("p c n -> p (c n)"), area["ga"][:], ACT.Copy)\
                            .then_inc(xt_hi_set[n], 1)
                    elif s == "Q":
                        for a, what, slot in (("gb", "q", Q_HI), ("ga", "k", K_HI)):
                            filled(act, it, a, what, *key)
                            for c in range(C):
                                act.activation(qk[n][:, c, slot, :], area[a][:, c * N:(c + 1) * N], ACT.Identity,
                                               bias=b_col[f"{what}{l}"][:, c:c + 1]).then_inc(qk_hi_set[n], 1)
                        if l == 1:
                            filled(act, it, "gb", "ca", *key)
                            act.activation(ca_hl[n][:, 0, :], area["gb"][0:2, 0:N], ACT.Identity, bias=bg_col[:])\
                                .then_inc(ca_hi_set[n], 1)
                    elif s == "M":
                        filled(act, it, "gb", "m", *key)
                        act.activation(m_hl[n][:, 0, :], area["gb"][0:H * T, 0:P], ACT.Copy).then_inc(m_hi_set[n], 1)
                    elif s == "E":
                        for c in range(2 * T):
                            t, grp = c % T, c // T
                            a = f"sc{c % 2}"
                            filled(act, it, a, f"e{c}", *key)
                            act.activation(probs[n][:, t, G * grp:G * (grp + 1), :].rearrange("p h n -> p (h n)"),
                                           area[a][:], ACT.Exp).then_inc(exped[n], 1)
                    elif s == "F" and l in LN:
                        act.wait_ge(ln_done[n], per_ln(it, l, 8) + 5)
                        act.activation(std[n][:], mv[n][:, :, 1], ACT.Sqrt, bias=eps_col[:]).then_inc(std_set[n], 1)
                    elif s == "G":
                        act.wait_ge(fp_set[n], per_step(it, T, T))
                        for t in range(T):
                            act.activation(dk[n][:, t, :], ident[:], ACT.Copy, scale=fp[n][:, t, D + 1:D + 2])\
                                .then_inc(dk_set[n], 1)
                    elif s == "W":
                        act.wait_ge(l2_done[n], per_step(it, 5, 4))
                        for t in range(T):
                            act.activation(p2[n][:, t, :], lk[n][:, t, :], ACT.Exp, bias=m2[n][:, t:t + 1],
                                           accum_out=s2[n][:, t:t + 1]).then_inc(p2_set[n], 1)
                        filled(act, it, "gb", "pt", *key)
                        act.activation(p2t[n][:].rearrange("p t n -> p (t n)"), area["gb"][:], ACT.Copy)\
                            .then_inc(p2t_set[n], 1)

        @block.vector
        def _(dve):
            dve.wait_ge(w_loaded, 16 * len(plain))
            dve.wait_ge(consts_set, CONSTS)
            for j in range(2):
                for c in range(C):
                    dve.tensor_tensor_reduce(junk[:], fc_ext[:, c, 0:D], w_qk2[:, j, :], 1.0, 0.0, ALU.mult, ALU.add,
                                             fc_ext[:, c, D + j:D + j + 1]).then_inc(fc_set, 1)
                    dve.wait_ge(fc_set, j * (C + 1) + c + 1)
                dve.tensor_tensor_reduce(junk[:], fc_row[:, 0:D], w_qk2[:, j, :], 1.0, 0.0, ALU.mult, ALU.add,
                                         fc_row[:, D + j:D + j + 1]).then_inc(fc_set, 1)
                dve.wait_ge(fc_set, j * (C + 1) + C + 1)
            dve.tensor_tensor(fc_row[:, D:D + 2], fc_row[:, D:D + 2], b_qk2[:], ALU.add).then_inc(fc_set, 1)
            dve.wait_ge(fc_set, FC_STEPS)
            for n, name in enumerate(names):
                if name == "fc":
                    src = fc_ext[:]
                    dve.tensor_copy(junk[:, 0:1], src[:, 0, 0:1]).then_inc(w_split, 1)
                else:
                    src = raw[:, n % 2]
                    dve.wait_ge(w_raw[n % 2], 16 * (n // 2 + 1))
                    dve.tensor_scalar(src, src, SCALE if name[0] == "q" else 1.0, None, ALU.mult).then_inc(w_split, 1)
                    dve.wait_ge(w_split, SPLIT_EACH * n + 1)
                dve.tensor_copy(w_hi[name][:], src).then_inc(w_split, 1)
                dve.wait_ge(w_split, SPLIT_EACH * n + 2)
                dve.tensor_tensor(w_lo[name][:], src, w_hi[name][:].bitcast(F32), ALU.subtract).then_inc(w_split, 1)

            with dve.Fori(0, STEPS) as it:
                for s, n, l in ORDER:
                    key = (n, l)
                    if s == "T":
                        dve.wait_ge(xt_hi_set[n], per_layer(it, l) + 1)
                        dve.tensor_tensor(xt_lo[n][:].rearrange("p c n -> p (c n)"), area["ga"][:],
                                          xt_hi[n][:].bitcast(F32).rearrange("p c n -> p (c n)"), ALU.subtract)\
                            .then_inc(xt_lo_set[n], 1)
                    elif s == "Q":
                        for i, (a, what, hi, lo) in enumerate((("gb", "q", Q_HI, Q_LO), ("ga", "k", K_HI, K_LO))):
                            dve.wait_ge(qk_hi_set[n], per_mha(it, l, 2 * C) + (i + 1) * C)
                            for c in range(C):
                                dve.scalar_tensor_tensor(out=qk[n][:, c, lo, :], in0=area[a][:, c * N:(c + 1) * N],
                                                         scalar=b_col[f"{what}{l}"][:, c:c + 1],
                                                         in1=qk[n][:, c, hi, :].bitcast(F32),
                                                         op0=ALU.add, op1=ALU.subtract).then_inc(qk_lo_set[n], 1)
                        if l == 1:
                            dve.wait_ge(ca_hi_set[n], per_step(it, 1, 1))
                            dve.scalar_tensor_tensor(out=ca_hl[n][:, 1, :], in0=area["gb"][0:2, 0:N], scalar=bg_col[:],
                                                     in1=ca_hl[n][:, 0, :].bitcast(F32), op0=ALU.add,
                                                     op1=ALU.subtract).then_inc(ca_lo_set[n], 1)
                    elif s == "V":
                        filled(dve, it, "gb", "v", *key)
                        bias = b_row[f"v{l}"][:].unsqueeze(1).to_broadcast([P, T, D])
                        dve.tensor_tensor(v_sb[n][:], area["gb"][:].rearrange("p (t d) -> p t d", t=T), bias, ALU.add)\
                            .then_inc(v_set[n], 1)
                    elif s == "S":
                        for c in range(2 * T):
                            t, grp = c % T, c // T
                            a = f"sc{c % 2}"
                            filled(dve, it, a, f"s{c}", *key)
                            dve.tensor_reduce(negm[n][:, G * grp:G * (grp + 1), t],
                                              area[a][:].rearrange("p (h n) -> p h n", h=G), AX_X, ALU.max,
                                              negate=True).then_inc(maxed[n], 1)
                    elif s == "M":
                        dve.wait_ge(m_hi_set[n], per_mha(it, l) + 1)
                        dve.tensor_tensor(m_hl[n][:, 1, :], area["gb"][0:H * T, 0:P], m_hl[n][:, 0, :].bitcast(F32),
                                          ALU.subtract).then_inc(m_lo_set[n], 1)
                    elif s == "O":
                        filled(dve, it, "den", "d", *key)
                        dve.reciprocal(rden[n][:].rearrange("p c n -> p (c n)"), area["den"][:]).then_inc(rden_set[n], 1)
                        dve.wait_ge(rden_set[n], per_mha(it, l) + 1)
                        filled(dve, it, "att", "o", *key)
                        dve.tensor_tensor(o_t[n][:].rearrange("p c n -> p (c n)"), area["att"][:],
                                          rden[n][:].rearrange("p c n -> p (c n)"), ALU.mult).then_inc(o_set[n], 1)
                    elif s == "F":
                        filled(dve, it, "ga", "f", *key)
                        src = area["ga"][:].rearrange("p (t d) -> p t d", t=T)
                        if l not in LN:
                            dve.tensor_tensor(xs[n][:], src, xs[n][:], ALU.add).then_inc(x_set[n], 1)
                            continue
                        done = per_ln(it, l, 8)
                        dve.wait_ge(xb_set[n], per_ln(it, l) + 1)
                        dve.tensor_tensor(h_sb[n][:], src, xb[n][:], ALU.add).then_inc(ln_done[n], 1)
                        dve.wait_ge(ln_done[n], done + 1)
                        for t in range(T):
                            dve.bn_stats(bn6[n][:, t, :], h_sb[n][:, t, :]).then_inc(ln_done[n], 1)
                        dve.wait_ge(ln_done[n], done + 3)
                        own_slot(dve)
                        for t in range(T):
                            dve.bn_aggr(mv[n][:, t, :], bn6[n][:, t, :]).then_inc(ln_done[n], 1)
                        dve.wait_ge(ln_done[n], done + 5)
                        for t in range(T):
                            dve.scalar_tensor_tensor(out=h_sb[n][:, t, :], in0=h_sb[n][:, t, :], scalar=mv[n][:, t, 0:1],
                                                     in1=b_row[f"g{l}"][:], op0=ALU.subtract, op1=ALU.mult)\
                                .then_inc(ln_done[n], 1)
                        dve.wait_ge(std_set[n], per_ln(it, l) + 1)
                        dve.reciprocal(rstd[n][:], std[n][:]).then_inc(ln_done[n], 1)
                        dve.wait_ge(ln_done[n], done + 8)
                        if l == 0:
                            dve.wait_ge(stored[n], per_step(it, 16, 0))
                        for t in range(T):
                            last = dve.scalar_tensor_tensor(out=xs[n][:, t, :], in0=h_sb[n][:, t, :],
                                                            scalar=rstd[n][:, t:t + 1], in1=b_row[f"e{l}"][:],
                                                            op0=ALU.mult, op1=ALU.add)
                        last.then_inc(x_set[n], 1)
                    elif s == "G":
                        for t, a in enumerate(("ga", "gb")):
                            filled(dve, it, a, f"fp{t}", *key)
                            dve.tensor_tensor(fp[n][:, t, :], area[a][:, 0:D + 2], fc_row[:], ALU.add)\
                                .then_inc(fp_set[n], 1)
                    elif s == "K":
                        dve.wait_ge(prepared[n], per_step(it, 5, 5))
                        dve.tensor_scalar(nb2[n][:], nb2[n][:], NEG_BIG, None, ALU.mult).then_inc(l2_done[n], 1)
                        dve.wait_ge(l2_done[n], per_step(it, 5, 1))
                        filled(dve, it, "ga", "kb", *key)
                        for t in range(T):
                            last = dve.scalar_tensor_tensor(out=lg[n][:, t, :], in0=area["ga"][:, 0:N],
                                                            scalar=fp[n][:, t, D:D + 1], in1=nb2[n][:, t, :],
                                                            op0=ALU.add, op1=ALU.add)
                        last.then_inc(l2_done[n], 1)
                        dve.wait_ge(l2_done[n], per_step(it, 5, 2))
                        dve.scalar_tensor_tensor(out=lk[n], in0=lg[n], scalar=SLOPE, in1=lg[n],
                                                 op0=ALU.mult, op1=ALU.max).then_inc(l2_done[n], 1)
                        dve.wait_ge(l2_done[n], per_step(it, 5, 3))
                        dve.tensor_reduce(m2[n][:], lk[n], AX_X, ALU.max, negate=True).then_inc(l2_done[n], 1)
                    elif s == "A":
                        dve.wait_ge(p2_set[n], per_step(it, T, T))
                        dve.reciprocal(r2[n][:], s2[n][:]).then_inc(l2_done[n], 1)
                        dve.wait_ge(l2_done[n], per_step(it, 5, 5))
                        filled(dve, it, "ga", "av", *key)
                        for t in range(T):
                            last = dve.scalar_tensor_tensor(out=xs[n][:, t, :], in0=area["ga"][:, t * D:(t + 1) * D],
                                                            scalar=r2[n][:, t:t + 1], in1=xs[n][:, t, :],
                                                            op0=ALU.mult, op1=ALU.add)
                        last.then_inc(x_set[n], 1)


def kernel(**inputs):
    import numpy as np
    import concourse.bacc as bacc
    from concourse.bass_utils import run_bass_kernel_spmd

    f = {k: np.asarray(v) for k, v in inputs.items()}

    def col(v):
        return np.ascontiguousarray(v.reshape(-1, P).T)

    arrays = {"x": f["x"], "adj": f["adj"], "adj_t": np.ascontiguousarray(f["adj"].transpose(0, 2, 1))}
    for l, prefix in ((0, "L0_gnn_W"), (3, "L3_gnn_W")):
        for m in "qkvo":
            arrays[f"w_{m}{l}"] = np.ascontiguousarray(f[prefix + m].T)
    for m in "qkv":
        arrays[f"w_{m}1"] = f[f"L1_gnn_W_{m}"]
    for l, prefix in ((0, "L0_gnn_b"), (1, "L1_gnn_b_"), (3, "L3_gnn_b")):
        for m in "qk":
            arrays[f"w_b{m}{l}"] = col(f[prefix + m])
        arrays[f"w_bv{l}"] = f[prefix + "v"].reshape(1, -1)
    for l in (0, 3):
        arrays[f"w_bo{l}"] = f[f"L{l}_gnn_bo"].reshape(1, -1)
        arrays[f"w_bg{l}"] = f[f"L{l}_gnn_gamma"].reshape(1, -1)
        arrays[f"w_be{l}"] = f[f"L{l}_gnn_beta"].reshape(1, -1)
    arrays["w_g1"] = np.ascontiguousarray(f["L1_gnn_w_g"].reshape(2, -1, P).transpose(2, 1, 0)).reshape(P, -1)
    arrays["w_bg"] = np.pad(f["L1_gnn_b_g"].reshape(1, 1), ((0, 1), (0, 0)))
    arrays["w_fc"] = f["L2_gnn_W_fc"]
    arrays["w_bfc"] = f["L2_gnn_b_fc"].reshape(1, -1)
    for m in "qk":
        arrays[f"w_w{m}2"] = f[f"L2_gnn_w_{m}"].reshape(1, -1)
        arrays[f"w_b{m}2"] = f[f"L2_gnn_b_{m}"].reshape(1, 1)

    nc = bacc.Bacc("TRN2", target_bir_lowering=False, num_devices=1)
    ap = {k: nc.dram_tensor(f"in_{k}", v.shape, mybir.dt.from_np(v.dtype), kind="ExternalInput").ap()
          for k, v in arrays.items()}
    out = nc.dram_tensor("out", f["x"].shape, F32, kind="ExternalOutput").ap()
    gnn_stack(nc, ap["x"], ap["adj"], ap["adj_t"], {k[2:]: v for k, v in ap.items() if k[:2] == "w_"}, out)
    r = run_bass_kernel_spmd(nc, [{f"in_{k}": v for k, v in arrays.items()}], core_ids=[0])
    return r.results[0]["out"]
```
